# Optimizing a Trainium2 kernel written in Bass

```python
import numpy as np
import jax
import jax.numpy as jnp

def _softmax(x, axis=-1):
    return jax.nn.softmax(x, axis=axis)

def _gelu(x):
    return jax.nn.gelu(x, approximate=True)

def _silu(x):
    return jax.nn.silu(x)

def _sigmoid(x):
    return jax.nn.sigmoid(x)

def _layernorm(x, axis=-1, eps=1e-05):
    m = jnp.mean(x, axis=axis, keepdims=True)
    v = jnp.var(x, axis=axis, keepdims=True)
    return (x - m) / jnp.sqrt(v + eps)

def _scatter_add(tgt, idx, src, axis=0):
    return tgt.at[idx].add(src)

def _segment_sum(src, seg, n):
    return jax.ops.segment_sum(src, seg, n)
kernel_name = 'mk_cond_resid_d1_seqx_r4_be2393'

def setup_inputs(seed: int=0):
    np.random.seed(seed)
    _w = jnp.asarray

    def _rec_inputs():
        import jax
        import jax.numpy as jnp
        _rk = jax.random.key(seed)
        x = -0.000125 + 0.9999 * jax.random.normal(jax.random.fold_in(_rk, 1), (128, 64, 1024), jnp.float32)
        _lenS = 64 - jax.random.randint(jax.random.fold_in(_rk, 7), (128,), 0, max(1, 64 // 4) + 1, jnp.int32)
        _lenS2 = 64 - jax.random.randint(jax.random.fold_in(_rk, 8), (128,), 0, max(1, 64 // 4) + 1, jnp.int32)
        itok_B_6_15 = jax.random.randint(jax.random.fold_in(_rk, 11), (128,), 6, 16, jnp.int32)
        return (x, itok_B_6_15)
    x, itok_B_6_15 = _rec_inputs()

    def _L0_cond_setup():
        import jax, jax.numpy as jnp
        import numpy as np
        B, S, D_IN, D_OUT = (4, 512, 1024, 1024)
        RANK, MAX_LORAS = (16, 32)
        key = jax.random.key(seed)
        ks = jax.random.split(key, 6)
        x = jax.random.normal(ks[0], (B, S, D_IN), dtype=jnp.float32)
        adapter_ids = jax.random.randint(ks[1], (B,), 0, MAX_LORAS)
        base_weight = jax.random.normal(ks[2], (D_OUT, D_IN), dtype=jnp.float32) * D_IN ** (-0.5)
        base_bias = jax.random.normal(ks[3], (D_OUT,), dtype=jnp.float32) * 0.01
        lora_A_w = jax.random.normal(ks[4], (MAX_LORAS, RANK, D_IN), dtype=jnp.float32) * D_IN ** (-0.5)
        lora_B_w = jax.random.normal(ks[5], (MAX_LORAS, D_OUT, RANK), dtype=jnp.float32) * RANK ** (-0.5)
        return {'x': x, 'adapter_ids': adapter_ids, 'base_weight': base_weight, 'base_bias': base_bias, 'lora_A_w': lora_A_w, 'lora_B_w': lora_B_w}
    _L0_cond_all = _L0_cond_setup()
    _L0_cond_in = {k: v for k, v in _L0_cond_all.items() if k in ('base_weight', 'base_bias', 'lora_A_w', 'lora_B_w')}
    del _L0_cond_all
    return {'x': x, 'itok_B_6_15': itok_B_6_15, 'L0_cond_base_weight': _L0_cond_in['base_weight'], 'L0_cond_base_bias': _L0_cond_in['base_bias'], 'L0_cond_lora_A_w': _L0_cond_in['lora_A_w'], 'L0_cond_lora_B_w': _L0_cond_in['lora_B_w']}

def reference(x, itok_B_6_15, L0_cond_base_weight, L0_cond_base_bias, L0_cond_lora_A_w, L0_cond_lora_B_w):
    import jax
    import jax.numpy as jnp

    def _L0_cond_ref(x, adapter_ids, base_weight, base_bias, lora_A_w, lora_B_w):
        import jax, jax.numpy as jnp
        import numpy as np
        B, S, D_IN, D_OUT = (4, 512, 1024, 1024)
        RANK, MAX_LORAS = (16, 32)
        result = jnp.einsum('bsd,od->bso', x, base_weight) + base_bias
        A = lora_A_w[adapter_ids]
        Bw = lora_B_w[adapter_ids]
        h = jnp.einsum('bsd,brd->bsr', x, A)
        lora_out = jnp.einsum('bsr,bor->bso', h, Bw)
        result = result + lora_out
        return result.astype(x.dtype)
    x = x + _L0_cond_ref(x, itok_B_6_15, L0_cond_base_weight, L0_cond_base_bias, L0_cond_lora_A_w, L0_cond_lora_B_w)
    return x

_drawn_inputs = setup_inputs


def setup_inputs(seed=0):
    import zlib

    import numpy as np

    out = dict(_drawn_inputs(seed))
    spreads = {}
    factors = {'L0_cond_base_bias': 8.0}
    for name, (base, spread) in spreads.items():
        noise = np.random.default_rng([zlib.crc32(name.encode()), seed]).standard_normal(out[name].shape)
        drawn = base * np.exp(spread * noise) if base else spread * noise
        out[name] = jnp.asarray(drawn.astype(out[name].dtype))
    for name, factor in factors.items():
        out[name] = (out[name] * factor).astype(out[name].dtype)
    return out
```

```python
from contextlib import ExitStack

import concourse.bass as bass
from concourse import mybir

P = 128
Q = 32
BANK = 512
ALU = mybir.AluOpType
F32 = mybir.dt.float32
F32R = mybir.dt.float32r
I32 = mybir.dt.int32
AX_X = mybir.AxisListType.X


def lora_residual(nc, x, ids, weight, bias, lora_a, lora_b, out):
    NSEQ, S, D = x.shape
    DOUT = weight.shape[0]
    NADAPT, R, _ = lora_a.shape
    NQ = P // Q
    DQ = D // NQ
    KT = DQ // Q
    SPT = P // S
    TILES = NSEQ // SPT
    XB = P // Q
    ROWS = P + SPT * R
    NW = DOUT // P
    NB = DOUT // BANK
    OPT = DOUT // Q
    assert SPT * R == Q and TILES % 2 == 0 and D == DOUT and OPT == Q

    x_rows = x.rearrange("n s d -> (n s) d")
    out_rows = out.rearrange("n s d -> (n s) d")

    with ExitStack() as ctx:
        def sb(name, shape, dt=F32):
            return ctx.enter_context(nc.sbuf_tensor(name, shape, dt))

        def psum(name, shape):
            return ctx.enter_context(nc.psum_tensor(name, shape, F32))

        def sem(name):
            return ctx.enter_context(nc.semaphore(name))

        w_raw = sb("w_raw", [P, NW, XB, DQ])
        w_turned = sb("w_turned", [P, 2, KT, P])
        w_high = sb("w_high", [P, KT, DOUT], F32R)
        w_low = sb("w_low", [P, KT, DOUT], F32R)
        rows_raw = sb("rows_raw", [P, 2, XB + 1, DQ])
        turned = sb("turned", [P, KT, ROWS])
        split = sb("split", [P, 2, 2, KT, ROWS], F32R)
        b_raw = sb("b_raw", [Q, 2, SPT, OPT * R])
        b_turned = sb("b_turned", [Q, DOUT])
        b_moving = sb("b_moving", [P, DOUT], F32R)
        h_sum = sb("h_sum", [P, Q])
        h_split = sb("h_split", [P, 3, Q], F32R)
        h_stat = sb("h_stat", [P, P], F32R)
        ident = sb("ident", [P, P])
        ident32 = sb("ident32", [P, Q])
        bias_all = sb("bias_all", [P, DOUT])
        result = sb("result", [P, 2, DOUT])
        ids_in = sb("ids_in", [1, NSEQ], I32)
        ids_f = sb("ids_f", [1, NSEQ])
        ids_neg = sb("ids_neg", [1, NSEQ])
        ids_ok = sb("ids_ok", [1, NSEQ], I32)

        acc = [[psum(f"acc{b}{n}", [P, BANK]) for n in range(NB)] for b in range(2)]
        h_acc = [psum(f"h_acc{b}", [P, BANK]) for b in range(2)]
        h_turned = psum("h_turned", [P, BANK])

        ids_landed = sem("ids_landed")
        bias_landed = sem("bias_landed")
        w_landed = [sem(f"w_landed{i}") for i in range(NW)]
        rows_landed = [sem(f"rows_landed{b}") for b in range(2)]
        b_landed = [sem(f"b_landed{b}") for b in range(2)]
        stored = [sem(f"stored{b}") for b in range(2)]
        zeroed = sem("zeroed")
        ident_ready = sem("ident_ready")
        ids_step = sem("ids_step")
        w_plus_i = sem("w_plus_i")
        w_is_turned = sem("w_is_turned")
        w_high_ready = sem("w_high_ready")
        w_ready = sem("w_ready")
        rows_turned = sem("rows_turned")
        high_ready = sem("high_ready")
        split_ready = sem("split_ready")
        base_done = sem("base_done")
        h_done = sem("h_done")
        h_summed = sem("h_summed")
        h_high_ready = sem("h_high_ready")
        h_split_ready = sem("h_split_ready")
        h_is_turned = sem("h_is_turned")
        h_stat_ready = sem("h_stat_ready")
        b_is_turned = sem("b_is_turned")
        b_high_ready = sem("b_high_ready")
        b_ready = sem("b_ready")
        lora_done = sem("lora_done")
        result_ready = sem("result_ready")

        X_DMAS = NQ + NQ * SPT

        def steps(one_step):
            def run(eng):
                with eng.Fori(1, TILES // 2 - 1) as pair:
                    one_step(2 * pair, 0, pair, True)
                    one_step(2 * pair + 1, 1, pair, True)
                one_step(TILES - 2, 0, TILES // 2 - 1, False)
                one_step(TILES - 1, 1, TILES // 2 - 1, False)
            return run

        block = ctx.enter_context(nc.Block())

        @block.sync
        def _(sp):
            def adapter(t, s):
                return sp.value_load(ids_ok[0:1, bass.ds(SPT * t + s, 1)], min_val=0, max_val=NADAPT - 1)

            def load_tokens(t, b):
                for q in range(NQ):
                    sp.dma_start(
                        rows_raw[Q * q:Q * q + Q, b, 0:XB, :],
                        x_rows[bass.ds(P * t, P), DQ * q:DQ * q + DQ].rearrange("(k p) c -> p k c", p=Q),
                    ).then_inc(rows_landed[b], 16)

            def load_a(t, b):
                for s in range(SPT):
                    a = adapter(t, s)
                    for q in range(NQ):
                        sp.dma_start(
                            rows_raw[Q * q + R * s:Q * q + R * s + R, b, XB, :],
                            lora_a[bass.ds(a, 1), :, DQ * q:DQ * q + DQ].rearrange("a r c -> (a r) c"),
                        ).then_inc(rows_landed[b], 16)

            def load_b(t, b):
                adapters = [adapter(t, s) for s in range(SPT)]
                if not isinstance(t, int) or t >= 2:
                    sp.wait_ge(b_is_turned, t - 1)
                for s in range(SPT):
                    sp.dma_start(
                        b_raw[:, b, s, :],
                        lora_b[bass.ds(adapters[s], 1)].rearrange("a (p o) r -> (a p) (o r)", p=Q),
                    ).then_inc(b_landed[b], 16)

            def store(t, b):
                sp.wait_ge(result_ready, t + 1)
                sp.dma_start(out_rows[bass.ds(P * t, P), :], result[:, b, :]).then_inc(stored[b], 16)

            sp.dma_start(ids_in[:, :], ids.rearrange("(a n) -> a n", a=1)).then_inc(ids_landed, 16)
            load_tokens(0, 0)
            load_tokens(1, 1)
            sp.wait_ge(ids_step, 4)
            load_a(0, 0)
            load_a(1, 1)
            load_b(0, 0)
            load_b(1, 1)
            sp.dma_start(bias_all[:, :], bias.rearrange("(a n) -> a n", a=1).partition_broadcast(P)
                         ).then_inc(bias_landed, 16)
            for t in range(2):
                sp.wait_ge(rows_turned, t + 1)
                load_tokens(t + 2, t)
                load_a(t + 2, t)
            load_b(2, 0)
            store(0, 0)

            def step(t, b, pair, full):
                if full:
                    sp.wait_ge(rows_turned, t + 1)
                    load_tokens(t + 2, b)
                    load_a(t + 2, b)
                if full or t == TILES - 2:
                    load_b(t + 1, 1 - b)
                store(t - 1, 1 - b)

            steps(step)(sp)
            store(TILES - 1, 1)
            for b in range(2):
                sp.wait_ge(stored[b], 16 * (TILES // 2))

        @block.gpsimd
        def _(pool):
            for tile in (ident, ident32):
                nc.gpsimd.memset(tile[:, :], 0.0).then_inc(zeroed, 1)
            pool.wait_ge(zeroed, 2)
            nc.gpsimd.affine_select(out=ident[:, :], in_=ident[:, :], compare_op=ALU.not_equal, fill=1.0,
                                    base=0, pattern=[[-1, P]], channel_multiplier=1).then_inc(ident_ready, 1)
            for q in range(NQ):
                nc.gpsimd.affine_select(out=ident32[:, :], in_=ident32[:, :], compare_op=ALU.not_equal,
                                        fill=1.0, base=-Q * q, pattern=[[-1, Q]],
                                        channel_multiplier=1).then_inc(ident_ready, 1)
                pool.wait_ge(ident_ready, q + 2)

        @block.scalar
        def _(act):
            def high_rows(t, b):
                act.wait_ge(rows_turned, t + 1)
                if not isinstance(t, int) or t >= 2:
                    act.wait_ge(base_done, t - 1)
                nc.scalar.copy(split[:, b, 0], turned[:, :, :]).then_inc(high_ready, 1)

            def high_b(t):
                act.wait_ge(b_is_turned, t + 1)
                if not isinstance(t, int) or t >= 1:
                    act.wait_ge(lora_done, t)
                nc.scalar.copy(b_moving[0:Q, :], b_turned[:, :])
                nc.scalar.copy(b_moving[Q:2 * Q, :], b_turned[:, :]).then_inc(b_high_ready, 1)

            def copy_h(t):
                act.wait_ge(h_is_turned, t + 1)
                nc.scalar.copy(h_stat[0:3 * Q, :], h_turned[0:3 * Q, 0:P]).then_inc(h_stat_ready, 1)

            def high_w(i):
                act.wait_ge(w_is_turned, i + 1)
                nc.scalar.copy(w_high[:, :, P * i:P * i + P], w_turned[:, i % 2]).then_inc(w_high_ready, 1)

            for i in range(NW):
                for q in range(NQ):
                    act.dma_start(
                        w_raw[Q * q:Q * q + Q, i],
                        weight[P * i:P * i + P, DQ * q:DQ * q + DQ].rearrange("(k p) c -> p k c", p=Q),
                    ).then_inc(w_landed[i], 16)
            high_w(0)
            high_rows(0, 0)
            high_w(1)
            high_rows(1, 1)
            for i in range(2, NW):
                high_w(i)
                if i == 4:
                    copy_h(0)
            high_b(0)
            high_rows(2, 0)
            high_b(1)

            def step(t, b, pair, full):
                if full or t == TILES - 2:
                    high_rows(t + 1, 1 - b)
                copy_h(t - 1)
                high_b(t)

            steps(step)(act)
            copy_h(TILES - 1)

        @block.tensor
        def _(pe):
            def h_products(t, b, k):
                nc.tensor.matmul(h_acc[b][:, 0:2 * Q], split[:, b, 0, k, 0:P], split[:, b, :, k, P:ROWS],
                                 start=(k == 0), stop=False, skip_group_check=True)

            def h_products_low(t, b, k):
                mm = nc.tensor.matmul(h_acc[b][:, 0:Q], split[:, b, 1, k, 0:P], split[:, b, 0, k, P:ROWS],
                                      start=False, stop=(k == KT - 1), skip_group_check=True)
                if k == KT - 1:
                    mm.then_inc(h_done, 1)

            def turn_h(t):
                pe.wait_ge(h_split_ready, t + 1)
                nc.tensor.transpose(h_turned[0:3 * Q, 0:P], h_split[:, :, :].bitcast(F32).rearrange("p a c -> p (a c)"),
                                    ident[:, :]).then_inc(h_is_turned, 1)

            def lora(t, b):
                pe.wait_ge(h_stat_ready, t + 1)
                pe.wait_ge(b_ready, t + 1)
                for n in range(NB):
                    mm = nc.tensor.matmul(acc[b][n][:, :], h_stat[0:3 * Q, :], b_moving[0:3 * Q, BANK * n:BANK * n + BANK],
                                          start=False, stop=True, skip_group_check=True)
                mm.then_inc(lora_done, 1)

            pe.wait_ge(ident_ready, 1)

            def panel(i, t):
                n, o = P * i // BANK, P * i % BANK
                for k in range(KT):
                    for lhs, w in ((0, w_high), (0, w_low), (1, w_high)):
                        mm = nc.tensor.matmul(acc[t][n][:, o:o + P], split[:, t, lhs, k, 0:P],
                                              w[:, k, P * i:P * i + P],
                                              start=(o == 0 and k == 0 and lhs == 0 and w is w_high),
                                              stop=False, skip_group_check=True)
                return mm

            for t in range(2):
                pe.wait_ge(split_ready, t + 1)
                for k in range(KT):
                    h_products(t, t, k)
                    h_products_low(t, t, k)
            for i in range(NW - 2):
                pe.wait_ge(w_ready, i + 1)
                panel(i, 0)
                panel(i, 1)
                if i == 2:
                    turn_h(0)
            pe.wait_ge(w_ready, NW)
            panel(NW - 2, 0)
            panel(NW - 1, 0).then_inc(base_done, 1)
            panel(NW - 2, 1)
            lora(0, 0)
            panel(NW - 1, 1).then_inc(base_done, 1)

            def step(t, b, pair, full):
                pe.wait_ge(split_ready, t + 1)
                pe.wait_ge(result_ready, t - 1)
                for k in range(KT):
                    for n in range(NB):
                        nc.tensor.matmul(acc[b][n][:, :], split[:, b, 0, k, 0:P], w_high[:, k, BANK * n:BANK * n + BANK],
                                         start=(k == 0), stop=False, skip_group_check=True)
                        nc.tensor.matmul(acc[b][n][:, :], split[:, b, 0, k, 0:P], w_low[:, k, BANK * n:BANK * n + BANK],
                                         start=False, stop=False, skip_group_check=True)
                    h_products(t, b, k)
                    h_products_low(t, b, k)
                    for n in range(NB):
                        mm = nc.tensor.matmul(acc[b][n][:, :], split[:, b, 1, k, 0:P], w_high[:, k, BANK * n:BANK * n + BANK],
                                              start=False, stop=False, skip_group_check=True)
                    if k == KT - 1:
                        mm.then_inc(base_done, 1)
                    if k == 2:
                        turn_h(t - 1)
                    if k == 4:
                        lora(t - 1, 1 - b)

            steps(step)(pe)
            turn_h(TILES - 1)
            lora(TILES - 1, 1)

        @block.vector
        def _(dve):
            def turn_rows(t, b, landed):
                dve.wait_ge(rows_landed[b], 16 * X_DMAS * landed)
                if not isinstance(t, int) or t >= 1:
                    dve.wait_ge(high_ready, t)
                nc.vector.transpose(
                    turned[:, :, :].rearrange("p j (k c) -> p k j c", c=Q),
                    rows_raw[:, b].rearrange("p k (j c) -> p k j c", c=Q),
                ).then_inc(rows_turned, 1)

            def low_rows(t, b):
                dve.wait_ge(high_ready, t + 1)
                nc.vector.tensor_tensor(split[:, b, 1], turned[:, :, :], split[:, b, 0].bitcast(F32),
                                        ALU.subtract).then_inc(split_ready, 1)

            def sum_h(t, b):
                dve.wait_ge(h_done, t + 1)
                if not isinstance(t, int) or t >= 1:
                    dve.wait_ge(h_is_turned, t)
                for s in range(SPT):
                    nc.vector.tensor_reduce(
                        h_sum[S * s:S * s + S, R * s:R * s + R],
                        h_acc[b][S * s:S * s + S, 0:2 * Q].rearrange("p (a c) -> p c a", a=2)[:, R * s:R * s + R, :],
                        AX_X, ALU.add).then_inc(h_summed, 1)
                dve.wait_ge(h_summed, SPT * (t + 1))
                nc.vector.tensor_copy(h_split[:, 0, :], h_sum[:, :])
                nc.vector.tensor_copy(h_split[:, 2, :], h_sum[:, :]).then_inc(h_high_ready, 1)
                dve.wait_ge(h_high_ready, t + 1)
                nc.vector.tensor_tensor(h_split[:, 1, :], h_sum[:, :], h_split[:, 0, :].bitcast(F32),
                                        ALU.subtract).then_inc(h_split_ready, 1)

            def turn_b(t, b, landed):
                dve.wait_ge(b_landed[b], 16 * SPT * landed)
                if not isinstance(t, int) or t >= 1:
                    dve.wait_ge(b_ready, t)
                nc.vector.transpose(
                    b_turned[:, :].rearrange("p (c o) -> p o c", c=Q),
                    b_raw[:, b].rearrange("p s (o r) -> p o s r", r=R),
                ).then_inc(b_is_turned, 1)

            def low_b(t):
                dve.wait_ge(b_high_ready, t + 1)
                nc.vector.tensor_tensor(b_moving[2 * Q:3 * Q, :], b_turned[:, :], b_moving[0:Q, :].bitcast(F32),
                                        ALU.subtract).then_inc(b_ready, 1)

            def finish(t, b, landed):
                dve.wait_ge(lora_done, t + 1)
                if not isinstance(t, int) or t >= 2:
                    dve.wait_ge(stored[b], 16 * landed)
                for n in range(NB):
                    ins = nc.vector.tensor_tensor(result[:, b, BANK * n:BANK * n + BANK], acc[b][n][:, :],
                                                  bias_all[:, BANK * n:BANK * n + BANK], ALU.add)
                ins.then_inc(result_ready, 1)

            def w_panel(i):
                dve.wait_ge(w_landed[i], 16 * NQ)
                q, c = P * i // DQ, P * i % DQ
                for k in range(XB):
                    at = w_raw[Q * q:Q * q + Q, i, k, c + Q * k:c + Q * k + Q]
                    nc.vector.tensor_tensor(at, at, ident32[Q * q:Q * q + Q, :], ALU.add).then_inc(w_plus_i, 1)
                dve.wait_ge(w_plus_i, XB * (i + 1))
                if i >= 2:
                    dve.wait_ge(w_ready, i - 1)
                nc.vector.transpose(
                    w_turned[:, i % 2].rearrange("p j (k c) -> p k j c", c=Q),
                    w_raw[:, i].rearrange("p k (j c) -> p k j c", c=Q),
                ).then_inc(w_is_turned, 1)

            def w_low_panel(i):
                dve.wait_ge(w_high_ready, i + 1)
                cols = slice(P * i, P * i + P)
                nc.vector.tensor_tensor(w_low[:, :, cols], w_turned[:, i % 2], w_high[:, :, cols].bitcast(F32),
                                        ALU.subtract).then_inc(w_ready, 1)

            dve.wait_ge(ids_landed, 16)
            nc.vector.tensor_copy(ids_f[:, :], ids_in[:, :]).then_inc(ids_step, 1)
            dve.wait_ge(ids_step, 1)
            nc.vector.tensor_scalar(ids_neg[:, :], ids_f[:, :], 0.0, float(NADAPT), ALU.is_lt, ALU.mult).then_inc(ids_step, 1)
            dve.wait_ge(ids_step, 2)
            nc.vector.tensor_tensor(ids_f[:, :], ids_f[:, :], ids_neg[:, :], ALU.add).then_inc(ids_step, 1)
            dve.wait_ge(ids_step, 3)
            nc.vector.tensor_scalar(ids_ok[:, :], ids_f[:, :], 0.0, float(NADAPT - 1), ALU.max, ALU.min).then_inc(ids_step, 1)
            nc.vector.memset(h_sum[:, :], 0.0)
            dve.wait_ge(ident_ready, 1 + NQ)
            w_panel(0)
            w_low_panel(0)
            turn_rows(0, 0, 1)
            low_rows(0, 0)
            w_panel(1)
            w_low_panel(1)
            turn_rows(1, 1, 1)
            low_rows(1, 1)
            for i in range(2, NW):
                w_panel(i)
                w_low_panel(i)
                if i == 2:
                    sum_h(0, 0)
            turn_b(0, 0, 1)
            low_b(0)
            turn_rows(2, 0, 2)
            low_rows(2, 0)
            finish(0, 0, 0)
            turn_b(1, 1, 1)
            low_b(1)

            def step(t, b, pair, full):
                sum_h(t - 1, 1 - b)
                if full or t == TILES - 2:
                    turn_rows(t + 1, 1 - b, pair + 1 + b)
                    low_rows(t + 1, 1 - b)
                finish(t - 1, 1 - b, pair - 1 + b)
                turn_b(t, b, pair + 1)
                low_b(t)

            steps(step)(dve)
            sum_h(TILES - 1, 1)
            finish(TILES - 1, 1, TILES // 2 - 1)


_INS = ["x", "itok_B_6_15", "L0_cond_base_weight", "L0_cond_base_bias", "L0_cond_lora_A_w", "L0_cond_lora_B_w"]


def kernel(**inputs):
    import numpy as np
    import concourse.bacc as bacc
    from concourse.bass_utils import run_bass_kernel_spmd

    nc = bacc.Bacc("TRN2", target_bir_lowering=False, num_devices=1)
    arrays, args = {}, []
    for name in _INS:
        a = np.ascontiguousarray(inputs[name])
        arrays[f"in_{name}"] = a
        args.append(nc.dram_tensor(f"in_{name}", a.shape, mybir.dt.from_np(a.dtype), kind="ExternalInput").ap())
    shape = arrays["in_x"].shape
    args.append(nc.dram_tensor("out", shape, F32, kind="ExternalOutput").ap())
    lora_residual(nc, *args)
    ran = run_bass_kernel_spmd(nc, [arrays], core_ids=[0])
    return ran.results[0]["out"]
```

```python
from contextlib import ExitStack

import concourse.bass as bass
from concourse import mybir

P = 128
Q = 32
GROUP = 256
ALU = mybir.AluOpType
F32 = mybir.dt.float32
F32R = mybir.dt.float32r
I32 = mybir.dt.int32


def lora_residual(nc, x, ids, weight, bias, lora_a, lora_b, out):
    NSEQ, S, D = x.shape
    DOUT = weight.shape[0]
    NADAPT, R, _ = lora_a.shape
    NQ = P // Q
    DQ = D // NQ
    KT = DQ // Q
    SPT = P // S
    TILES = NSEQ // SPT
    XB = P // Q
    NG = DOUT // GROUP
    PPG = GROUP // P
    NW = DOUT // P
    OPT = DOUT // Q
    SIDE = DOUT - GROUP
    COLS = DOUT + 2 * Q
    assert SPT * R == Q and TILES % 2 == 0 and D == DOUT and OPT == Q and NG == 4

    def at(o):
        return o if o < SIDE else o + Q

    A_AT = (SIDE, SIDE + Q + GROUP)
    PIECES = [
        [(0, 2 * GROUP, 0, 0), (2 * GROUP, GROUP, 2 * GROUP, 0), (SIDE, GROUP + Q, SIDE, Q)],
        [(0, 2 * GROUP, 0, 0), (2 * GROUP, GROUP, 2 * GROUP, 0), (SIDE + Q, GROUP + Q, SIDE, 0)],
    ]
    H_AT = (0, GROUP)
    OUT_N = (2 * GROUP, GROUP, GROUP)
    GROUP_ORDER = [0, NG - 1, 1, 2]
    PANEL_ORDER = [PPG * g + i for g in GROUP_ORDER for i in range(PPG)]

    x_rows = x.rearrange("n s d -> (n s) d")
    out_rows = out.rearrange("n s d -> (n s) d")

    with ExitStack() as ctx:
        def sb(name, shape, dt=F32):
            return ctx.enter_context(nc.sbuf_tensor(name, shape, dt))

        def psum(name, shape):
            return ctx.enter_context(nc.psum_tensor(name, shape, F32))

        def sem(name):
            return ctx.enter_context(nc.semaphore(name))

        w_raw = sb("w_raw", [P, NW, XB, DQ])
        w_turned = sb("w_turned", [P, 2, KT, P])
        w_high = sb("w_high", [P, KT, COLS], F32R)
        w_low = sb("w_low", [P, KT, COLS], F32R)
        x_raw = sb("x_raw", [P, 2, XB, DQ])
        x_turned = sb("x_turned", [P, KT, P])
        x_split = sb("x_split", [P, 2, 2, KT, P], F32R)
        a_raw = sb("a_raw", [P, 2, DQ])
        a_turned = sb("a_turned", [P, KT, Q])
        b_raw = sb("b_raw", [Q, 2, SPT, OPT * R])
        b_turned = sb("b_turned", [Q, DOUT])
        b_moving = sb("b_moving", [P, DOUT], F32R)
        h_split = sb("h_split", [P, 3, Q], F32R)
        h_stat = sb("h_stat", [P, P], F32R)
        ident = sb("ident", [P, P])
        ident32 = sb("ident32", [P, Q])
        bias_all = sb("bias_all", [P, DOUT])
        result = sb("result", [P, 2, DOUT])
        ids_in = sb("ids_in", [1, NSEQ], I32)
        ids_f = sb("ids_f", [1, NSEQ])
        ids_neg = sb("ids_neg", [1, NSEQ])
        ids_ok = sb("ids_ok", [1, NSEQ], I32)

        acc = [[psum(f"acc{b}{n}", [P, 2 * GROUP]) for n in range(3)] for b in range(2)]
        h_turned = psum("h_turned", [P, 2 * GROUP])

        ids_landed = sem("ids_landed")
        bias_landed = sem("bias_landed")
        w_landed = [sem(f"w_landed{g}") for g in range(NG)]
        x_landed = [sem(f"x_landed{b}") for b in range(2)]
        a_landed = [sem(f"a_landed{b}") for b in range(2)]
        b_landed = [sem(f"b_landed{b}") for b in range(2)]
        stored = [sem(f"stored{b}") for b in range(2)]
        zeroed = sem("zeroed")
        h_zeroed = sem("h_zeroed")
        ident_ready = sem("ident_ready")
        ids_step = sem("ids_step")
        w_plus_i = sem("w_plus_i")
        w_is_turned = sem("w_is_turned")
        w_high_ready = sem("w_high_ready")
        w_ready = sem("w_ready")
        x_is_turned = sem("x_is_turned")
        x_high_ready = sem("x_high_ready")
        x_ready = sem("x_ready")
        a_is_turned = sem("a_is_turned")
        a_high_ready = sem("a_high_ready")
        a_ready = sem("a_ready")
        b_is_turned = sem("b_is_turned")
        b_high_ready = sem("b_high_ready")
        b_ready = sem("b_ready")
        h_done = sem("h_done")
        h_high_ready = sem("h_high_ready")
        h_split_ready = sem("h_split_ready")
        h_is_turned = sem("h_is_turned")
        h_stat_ready = sem("h_stat_ready")
        base_done = sem("base_done")
        lora_done = sem("lora_done")
        result_ready = sem("result_ready")

        def from_tile(first, t):
            return not isinstance(t, int) or t >= first

        def steps(eng, one_step):
            with eng.Fori(1, TILES // 2 - 1) as pair:
                one_step(2 * pair, 0, pair, True, True)
                one_step(2 * pair + 1, 1, pair, True, True)
            one_step(TILES - 2, 0, TILES // 2 - 1, False, True)
            one_step(TILES - 1, 1, TILES // 2 - 1, False, False)

        block = ctx.enter_context(nc.Block())

        def load_w(eng, g):
            for q in range(NQ):
                eng.dma_start(
                    w_raw[Q * q:Q * q + Q, PPG * g:PPG * g + PPG].rearrange("p i k c -> p (i k) c"),
                    weight[GROUP * g:GROUP * g + GROUP, DQ * q:DQ * q + DQ].rearrange("(k p) c -> p k c", p=Q),
                ).then_inc(w_landed[g], 16)

        @block.sync
        def _(sp):
            def adapters(t):
                return [sp.value_load(ids_ok[0:1, bass.ds(SPT * t + s, 1)], min_val=0, max_val=NADAPT - 1)
                        for s in range(SPT)]

            def load_x(t, b):
                if from_tile(2, t):
                    sp.wait_ge(x_is_turned, t - 1)
                for q in range(NQ):
                    sp.dma_start(
                        x_raw[Q * q:Q * q + Q, b],
                        x_rows[bass.ds(P * t, P), DQ * q:DQ * q + DQ].rearrange("(k p) c -> p k c", p=Q),
                    ).then_inc(x_landed[b], 16)

            def load_a(t, b):
                chosen = adapters(t)
                if from_tile(2, t):
                    sp.wait_ge(a_is_turned, t - 1)
                for s in range(SPT):
                    for q in range(NQ):
                        sp.dma_start(
                            a_raw[Q * q + R * s:Q * q + R * s + R, b, :],
                            lora_a[bass.ds(chosen[s], 1), :, DQ * q:DQ * q + DQ].rearrange("a r c -> (a r) c"),
                        ).then_inc(a_landed[b], 16)

            def load_b(t, b):
                chosen = adapters(t)
                if from_tile(2, t):
                    sp.wait_ge(b_is_turned, t - 1)
                for s in range(SPT):
                    sp.dma_start(
                        b_raw[:, b, s, :],
                        lora_b[bass.ds(chosen[s], 1)].rearrange("a (p o) r -> (a p) (o r)", p=Q),
                    ).then_inc(b_landed[b], 16)

            def store(t, b):
                sp.wait_ge(result_ready, t + 1)
                sp.dma_start(out_rows[bass.ds(P * t, P), :], result[:, b, :]).then_inc(stored[b], 16)

            load_x(0, 0)
            sp.dma_start(ids_in[:, :], ids.rearrange("(a n) -> a n", a=1)).then_inc(ids_landed, 16)
            load_x(1, 1)
            sp.wait_ge(ids_step, 4)
            load_a(0, 0)
            load_a(1, 1)
            load_w(sp, GROUP_ORDER[2])
            load_w(sp, GROUP_ORDER[3])
            load_b(0, 0)
            load_b(1, 1)
            sp.dma_start(bias_all[:, :], bias.rearrange("(a n) -> a n", a=1).to_broadcast([P, DOUT])
                         ).then_inc(bias_landed, 16)
            load_x(2, 0)
            load_x(3, 1)
            load_a(2, 0)
            load_a(3, 1)
            load_b(2, 0)
            store(0, 0)

            def step(t, b, pair, two_more, one_more):
                if two_more:
                    load_x(t + 2, b)
                    load_a(t + 2, b)
                if one_more:
                    load_b(t + 1, 1 - b)
                store(t - 1, 1 - b)

            steps(sp, step)
            store(TILES - 1, 1)
            for b in range(2):
                sp.wait_ge(stored[b], 16 * (TILES // 2))

        @block.gpsimd
        def _(pool):
            for tile in (ident, ident32):
                nc.gpsimd.memset(tile[:, :], 0.0).then_inc(zeroed, 1)
            nc.gpsimd.memset(h_split[:, :, :].bitcast(F32), 0.0).then_inc(h_zeroed, 1)
            pool.wait_ge(zeroed, 2)
            for q in range(NQ):
                nc.gpsimd.affine_select(out=ident32[:, :], in_=ident32[:, :], compare_op=ALU.not_equal,
                                        fill=1.0, base=-Q * q, pattern=[[-1, Q]],
                                        channel_multiplier=1).then_inc(ident_ready, 1)
                pool.wait_ge(ident_ready, q + 1)
            nc.gpsimd.affine_select(out=ident[:, :], in_=ident[:, :], compare_op=ALU.not_equal, fill=1.0,
                                    base=0, pattern=[[-1, P]], channel_multiplier=1).then_inc(ident_ready, 1)
            pool.wait_ge(ident_ready, NQ + 1)
            for n, i in enumerate(PANEL_ORDER):
                if n % PPG == 0:
                    if n > 0:
                        pool.wait_ge(w_plus_i, XB * n)
                    pool.wait_ge(w_landed[i // PPG], 16 * NQ)
                q, c = P * i // DQ, P * i % DQ
                for k in range(XB):
                    diagonal = w_raw[Q * q:Q * q + Q, i, k, c + Q * k:c + Q * k + Q]
                    nc.gpsimd.tensor_tensor(diagonal, diagonal, ident32[Q * q:Q * q + Q, :],
                                            ALU.add).then_inc(w_plus_i, 1)

        @block.scalar
        def _(act):
            def high_x(t, b):
                act.wait_ge(x_is_turned, t + 1)
                if from_tile(2, t):
                    act.wait_ge(base_done, t - 1)
                nc.scalar.copy(x_split[:, b, 0], x_turned[:, :, :]).then_inc(x_high_ready, 1)

            def high_a(t, b):
                act.wait_ge(a_is_turned, t + 1)
                if from_tile(2, t):
                    act.wait_ge(base_done, t - 1)
                nc.scalar.copy(w_high[:, :, A_AT[b]:A_AT[b] + Q], a_turned[:, :, :]).then_inc(a_high_ready, 1)

            def high_b(t):
                act.wait_ge(b_is_turned, t + 1)
                if from_tile(1, t):
                    act.wait_ge(lora_done, t)
                nc.scalar.copy(b_moving[0:Q, :], b_turned[:, :])
                nc.scalar.copy(b_moving[Q:2 * Q, :], b_turned[:, :]).then_inc(b_high_ready, 1)

            def copy_h(t):
                act.wait_ge(h_is_turned, t + 1)
                nc.scalar.copy(h_stat[0:3 * Q, :], h_turned[0:3 * Q, 0:P]).then_inc(h_stat_ready, 1)

            def high_w(n):
                i = PANEL_ORDER[n]
                act.wait_ge(w_is_turned, n + 1)
                nc.scalar.copy(w_high[:, :, at(P * i):at(P * i) + P], w_turned[:, n % 2]).then_inc(w_high_ready, 1)

            load_w(act, GROUP_ORDER[0])
            load_w(act, GROUP_ORDER[1])
            high_x(0, 0)
            high_w(0)
            high_w(1)
            high_x(1, 1)
            high_a(0, 0)
            high_a(1, 1)
            for n in range(2, NW):
                high_w(n)
            copy_h(0)
            high_b(0)
            high_x(2, 0)
            high_a(2, 0)
            high_b(1)

            def step(t, b, pair, two_more, one_more):
                if one_more:
                    high_x(t + 1, 1 - b)
                    high_a(t + 1, 1 - b)
                copy_h(t - 1)
                high_b(t)

            steps(act, step)
            copy_h(TILES - 1)

        @block.tensor
        def _(pe):
            PASSES = ((0, w_high), (0, w_low), (1, w_high))

            def turn_h(t):
                pe.wait_ge(h_split_ready, t + 1)
                nc.tensor.transpose(h_turned[0:3 * Q, 0:P],
                                    h_split[:, :, :].bitcast(F32).rearrange("p a c -> p (a c)"),
                                    ident[:, :]).then_inc(h_is_turned, 1)

            def lora(t, b):
                pe.wait_ge(h_stat_ready, t + 1)
                pe.wait_ge(b_ready, t + 1)
                for n, (_, _, first, begin) in enumerate(PIECES[b]):
                    mm = nc.tensor.matmul(acc[b][n][:, begin:begin + OUT_N[n]], h_stat[0:3 * Q, :],
                                          b_moving[0:3 * Q, first:first + OUT_N[n]],
                                          start=False, stop=True, skip_group_check=True)
                mm.then_inc(lora_done, 1)

            def group(g, t):
                n = {0: 0, 1: 0, 2: 1, 3: 2}[g]
                col, width = (PIECES[t][2][0:2] if g == NG - 1 else (GROUP * g, GROUP))
                begin = GROUP * (g % 2) if n == 0 else 0
                for k in range(KT):
                    for part, w in PASSES:
                        mm = nc.tensor.matmul(acc[t][n][:, begin:begin + width], x_split[:, t, part, k, :],
                                              w[:, k, col:col + width],
                                              start=(begin == 0 and k == 0 and part == 0 and w is w_high),
                                              stop=False, skip_group_check=True)
                return mm

            pe.wait_ge(w_ready, PPG)
            for t in range(2):
                pe.wait_ge(x_ready, t + 1)
                group(GROUP_ORDER[0], t)
            pe.wait_ge(w_ready, 2 * PPG)
            for t in range(2):
                pe.wait_ge(a_ready, t + 1)
                group(GROUP_ORDER[1], t).then_inc(h_done, 1)
            pe.wait_ge(w_ready, 3 * PPG)
            group(GROUP_ORDER[2], 0)
            group(GROUP_ORDER[2], 1)
            pe.wait_ge(ident_ready, NQ + 1)
            turn_h(0)
            pe.wait_ge(w_ready, 4 * PPG)
            group(GROUP_ORDER[3], 0).then_inc(base_done, 1)
            lora(0, 0)
            group(GROUP_ORDER[3], 1).then_inc(base_done, 1)

            def step(t, b, pair, two_more, one_more):
                pe.wait_ge(x_ready, t + 1)
                pe.wait_ge(a_ready, t + 1)
                pe.wait_ge(result_ready, t - 1)
                for k in range(KT):
                    for part, w in PASSES:
                        for n, (col, width, _, _) in enumerate(PIECES[b]):
                            mm = nc.tensor.matmul(acc[b][n][:, 0:width], x_split[:, b, part, k, :],
                                                  w[:, k, col:col + width],
                                                  start=(k == 0 and part == 0 and w is w_high),
                                                  stop=False, skip_group_check=True)
                    if k == KT - 1:
                        mm.then_inc(base_done, 1)
                    if k == 2:
                        turn_h(t - 1)
                    if k == 4:
                        lora(t - 1, 1 - b)

            steps(pe, step)
            turn_h(TILES - 1)
            lora(TILES - 1, 1)

        @block.vector
        def _(dve):
            def turn_x(t, b, landed):
                dve.wait_ge(x_landed[b], 16 * NQ * landed)
                if from_tile(1, t):
                    dve.wait_ge(x_ready, t)
                nc.vector.transpose(
                    x_turned[:, :, :].rearrange("p j (k c) -> p k j c", c=Q),
                    x_raw[:, b].rearrange("p k (j c) -> p k j c", c=Q),
                ).then_inc(x_is_turned, 1)

            def low_x(t, b):
                dve.wait_ge(x_high_ready, t + 1)
                nc.vector.tensor_tensor(x_split[:, b, 1], x_turned[:, :, :], x_split[:, b, 0].bitcast(F32),
                                        ALU.subtract).then_inc(x_ready, 1)

            def turn_a(t, b, landed):
                dve.wait_ge(a_landed[b], 16 * NQ * SPT * landed)
                if from_tile(1, t):
                    dve.wait_ge(a_ready, t)
                nc.vector.transpose(a_turned[:, :, :].rearrange("p j c -> p (j c)"),
                                    a_raw[:, b, :]).then_inc(a_is_turned, 1)

            def low_a(t, b):
                dve.wait_ge(a_high_ready, t + 1)
                cols = slice(A_AT[b], A_AT[b] + Q)
                nc.vector.tensor_tensor(w_low[:, :, cols], a_turned[:, :, :], w_high[:, :, cols].bitcast(F32),
                                        ALU.subtract).then_inc(a_ready, 1)

            def split_h(t, b):
                dve.wait_ge(h_done if isinstance(t, int) and t < 2 else base_done, t + 1)
                if from_tile(1, t):
                    dve.wait_ge(h_is_turned, t)

                def own(s):
                    own_h = acc[b][2][S * s:S * s + S, H_AT[b] + R * s:H_AT[b] + R * s + R]
                    return own_h, h_split[S * s:S * s + S, :, R * s:R * s + R]

                for s in range(SPT):
                    own_h, parts = own(s)
                    for part in (0, 2):
                        nc.vector.tensor_copy(parts[:, part, :], own_h).then_inc(h_high_ready, 1)
                dve.wait_ge(h_high_ready, 2 * SPT * (t + 1))
                for s in range(SPT):
                    own_h, parts = own(s)
                    ins = nc.vector.tensor_tensor(parts[:, 1, :], own_h, parts[:, 0, :].bitcast(F32), ALU.subtract)
                ins.then_inc(h_split_ready, 1)

            def turn_b(t, b, landed):
                dve.wait_ge(b_landed[b], 16 * SPT * landed)
                if from_tile(1, t):
                    dve.wait_ge(b_ready, t)
                nc.vector.transpose(
                    b_turned[:, :].rearrange("p (c o) -> p o c", c=Q),
                    b_raw[:, b].rearrange("p s (o r) -> p o s r", r=R),
                ).then_inc(b_is_turned, 1)

            def low_b(t):
                dve.wait_ge(b_high_ready, t + 1)
                nc.vector.tensor_tensor(b_moving[2 * Q:3 * Q, :], b_turned[:, :], b_moving[0:Q, :].bitcast(F32),
                                        ALU.subtract).then_inc(b_ready, 1)

            def finish(t, b, landed):
                dve.wait_ge(lora_done, t + 1)
                if from_tile(2, t):
                    dve.wait_ge(stored[b], 16 * landed)
                for n, (_, _, first, begin) in enumerate(PIECES[b]):
                    cols = slice(first, first + OUT_N[n])
                    ins = nc.vector.tensor_tensor(result[:, b, cols], acc[b][n][:, begin:begin + OUT_N[n]],
                                                  bias_all[:, cols], ALU.add)
                ins.then_inc(result_ready, 1)

            def turn_w(n):
                i = PANEL_ORDER[n]
                dve.wait_ge(w_plus_i, XB * (n + 1))
                if n >= 2:
                    dve.wait_ge(w_ready, n - 1)
                nc.vector.transpose(
                    w_turned[:, n % 2].rearrange("p j (k c) -> p k j c", c=Q),
                    w_raw[:, i].rearrange("p k (j c) -> p k j c", c=Q),
                ).then_inc(w_is_turned, 1)

            def low_w(n):
                i = PANEL_ORDER[n]
                dve.wait_ge(w_high_ready, n + 1)
                cols = slice(at(P * i), at(P * i) + P)
                nc.vector.tensor_tensor(w_low[:, :, cols], w_turned[:, n % 2], w_high[:, :, cols].bitcast(F32),
                                        ALU.subtract).then_inc(w_ready, 1)

            turn_x(0, 0, 1)
            dve.wait_ge(ids_landed, 16)
            nc.vector.tensor_copy(ids_f[:, :], ids_in[:, :]).then_inc(ids_step, 1)
            dve.wait_ge(ids_step, 1)
            nc.vector.tensor_scalar(ids_neg[:, :], ids_f[:, :], 0.0, float(NADAPT), ALU.is_lt, ALU.mult).then_inc(ids_step, 1)
            dve.wait_ge(ids_step, 2)
            nc.vector.tensor_tensor(ids_f[:, :], ids_f[:, :], ids_neg[:, :], ALU.add).then_inc(ids_step, 1)
            dve.wait_ge(ids_step, 3)
            nc.vector.tensor_scalar(ids_ok[:, :], ids_f[:, :], 0.0, float(NADAPT - 1), ALU.max, ALU.min).then_inc(ids_step, 1)
            low_x(0, 0)
            turn_w(0)
            turn_w(1)
            low_w(0)
            low_w(1)
            turn_x(1, 1, 1)
            turn_a(0, 0, 1)
            low_x(1, 1)
            low_a(0, 0)
            turn_a(1, 1, 1)
            low_a(1, 1)
            for n in range(2, NW):
                turn_w(n)
                low_w(n)
            dve.wait_ge(h_zeroed, 1)
            split_h(0, 0)
            turn_b(0, 0, 1)
            low_b(0)
            turn_x(2, 0, 2)
            turn_a(2, 0, 2)
            low_x(2, 0)
            low_a(2, 0)
            dve.wait_ge(bias_landed, 16)
            finish(0, 0, 0)
            turn_b(1, 1, 1)
            low_b(1)

            def step(t, b, pair, two_more, one_more):
                split_h(t - 1, 1 - b)
                if one_more:
                    turn_x(t + 1, 1 - b, pair + 1 + b)
                    turn_a(t + 1, 1 - b, pair + 1 + b)
                    low_x(t + 1, 1 - b)
                    low_a(t + 1, 1 - b)
                finish(t - 1, 1 - b, pair - 1 + b)
                turn_b(t, b, pair + 1)
                low_b(t)

            steps(dve, step)
            split_h(TILES - 1, 1)
            finish(TILES - 1, 1, TILES // 2 - 1)


_INS = ["x", "itok_B_6_15", "L0_cond_base_weight", "L0_cond_base_bias", "L0_cond_lora_A_w", "L0_cond_lora_B_w"]


def kernel(**inputs):
    import numpy as np
    import concourse.bacc as bacc
    from concourse.bass_utils import run_bass_kernel_spmd

    nc = bacc.Bacc("TRN2", target_bir_lowering=False, num_devices=1)
    arrays, args = {}, []
    for name in _INS:
        a = np.ascontiguousarray(inputs[name])
        arrays[f"in_{name}"] = a
        args.append(nc.dram_tensor(f"in_{name}", a.shape, mybir.dt.from_np(a.dtype), kind="ExternalInput").ap())
    shape = arrays["in_x"].shape
    args.append(nc.dram_tensor("out", shape, F32, kind="ExternalOutput").ap())
    lora_residual(nc, *args)
    ran = run_bass_kernel_spmd(nc, [arrays], core_ids=[0])
    return ran.results[0]["out"]
```

```python
from contextlib import ExitStack

import concourse.bass as bass
from concourse import mybir

P = 128
Q = 32
GROUP = 256
ALU = mybir.AluOpType
F32 = mybir.dt.float32
F32R = mybir.dt.float32r
I32 = mybir.dt.int32


def lora_residual(nc, x, ids, weight, bias, lora_a, lora_b, out):
    NSEQ, S, D = x.shape
    DOUT = weight.shape[0]
    NADAPT, R, _ = lora_a.shape
    NQ = P // Q
    DQ = D // NQ
    KT = DQ // Q
    SPT = P // S
    TILES = NSEQ // SPT
    XB = P // Q
    NG = DOUT // GROUP
    PPG = GROUP // P
    NW = DOUT // P
    OPT = DOUT // Q
    SIDE = DOUT - GROUP
    COLS = DOUT + 2 * Q
    WBUFS = 4
    POOL_PANELS = (5, 7)
    assert min(POOL_PANELS) >= WBUFS and NW == 2 * WBUFS
    assert SPT * R == Q and TILES % 2 == 0 and D == DOUT and OPT == Q and NG == 4

    def at(o):
        return o if o < SIDE else o + Q

    A_AT = (SIDE, SIDE + Q + GROUP)
    PIECES = [
        [(0, 2 * GROUP, 0, 0), (2 * GROUP, GROUP, 2 * GROUP, 0), (SIDE, GROUP + Q, SIDE, Q)],
        [(0, 2 * GROUP, 0, 0), (2 * GROUP, GROUP, 2 * GROUP, 0), (SIDE + Q, GROUP + Q, SIDE, 0)],
    ]
    H_AT = (0, GROUP)
    OUT_N = (2 * GROUP, GROUP, GROUP)
    FIRST_H = (0, 1, TILES - 1)
    GROUP_ORDER = [0, NG - 1, 1, 2]
    LAST_ORDER = (2, 0, 1)
    PANEL_ORDER = [PPG * g + i for g in GROUP_ORDER for i in range(PPG)]

    x_rows = x.rearrange("n s d -> (n s) d")
    out_rows = out.rearrange("n s d -> (n s) d")

    with ExitStack() as ctx:
        def sb(name, shape, dt=F32):
            return ctx.enter_context(nc.sbuf_tensor(name, shape, dt))

        def psum(name, shape):
            return ctx.enter_context(nc.psum_tensor(name, shape, F32))

        def sem(name):
            return ctx.enter_context(nc.semaphore(name))

        w_raw = sb("w_raw", [P, NW, XB, DQ])
        w_turned = sb("w_turned", [P, WBUFS, KT, P])
        w_high = sb("w_high", [P, KT, COLS], F32R)
        w_low = sb("w_low", [P, KT, COLS], F32R)
        x_raw = sb("x_raw", [P, 2, XB, DQ])
        x_turned = sb("x_turned", [P, KT, P])
        x_split = sb("x_split", [P, 2, 2, KT, P], F32R)
        a_raw = sb("a_raw", [P, 2, SPT, R * D // P])
        a_turned = sb("a_turned", [P, 2, KT, Q])
        b_raw = sb("b_raw", [Q, 2, SPT, OPT * R])
        b_turned = sb("b_turned", [Q, DOUT])
        b_moving = sb("b_moving", [P, DOUT], F32R)
        h_split = sb("h_split", [P, 3, Q], F32R)
        h_stat = sb("h_stat", [P, P], F32R)
        ident = sb("ident", [P, P])
        warm = sb("warm", [1, 2])
        ident32 = sb("ident32", [P, Q])
        bias_all = sb("bias_all", [P, DOUT])
        result = sb("result", [P, 2, DOUT])
        ids_in = sb("ids_in", [1, NSEQ], I32)
        ids_f = sb("ids_f", [1, NSEQ])
        ids_neg = sb("ids_neg", [1, NSEQ])
        ids_ok = sb("ids_ok", [1, NSEQ], I32)

        acc = [[psum(f"acc{b}{n}", [P, 2 * GROUP]) for n in range(3)] for b in range(2)]
        h_turned = psum("h_turned", [P, 2 * GROUP])

        ids_landed = sem("ids_landed")
        bias_landed = sem("bias_landed")
        w_landed = [sem(f"w_landed{i}") for i in range(NW)]
        x_landed = [sem(f"x_landed{b}") for b in range(2)]
        a_landed = [sem(f"a_landed{b}") for b in range(2)]
        b_landed = [sem(f"b_landed{b}") for b in range(2)]
        stored = [sem(f"stored{b}") for b in range(2)]
        stored_last = sem("stored_last")
        zeroed = sem("zeroed")
        warm_zeroed = sem("warm_zeroed")
        h_zeroed = sem("h_zeroed")
        ident_ready = sem("ident_ready")
        ids_step = sem("ids_step")
        w_plus_i = sem("w_plus_i")
        w_is_turned = sem("w_is_turned")
        w_high_ready = sem("w_high_ready")
        w_ready = sem("w_ready")
        w_ready_pool = sem("w_ready_pool")
        x_is_turned = sem("x_is_turned")
        x_high_ready = sem("x_high_ready")
        x_ready = sem("x_ready")
        a_is_turned = sem("a_is_turned")
        a_high_ready = sem("a_high_ready")
        a_ready = sem("a_ready")
        b_is_turned = sem("b_is_turned")
        b_high_ready = sem("b_high_ready")
        b_ready = sem("b_ready")
        h_done = sem("h_done")
        h_high_ready = sem("h_high_ready")
        h_split_ready = sem("h_split_ready")
        h_is_turned = sem("h_is_turned")
        h_stat_ready = sem("h_stat_ready")
        base_done = sem("base_done")
        lora_done = sem("lora_done")
        last_bank_done = sem("last_bank_done")
        last_bank_ready = sem("last_bank_ready")
        result_ready = sem("result_ready")

        def from_tile(first, t):
            return not isinstance(t, int) or t >= first

        def steps(eng, one_step):
            one_step(2, 0, 1, True)
            one_step(3, 1, 1, True)
            with eng.Fori(2, TILES // 2 - 1) as pair:
                one_step(2 * pair, 0, pair, True)
                one_step(2 * pair + 1, 1, pair, True)
            one_step(TILES - 2, 0, TILES // 2 - 1, False)

        block = ctx.enter_context(nc.Block())

        def load_w(eng, g):
            for q in range(NQ):
                eng.dma_start(
                    w_raw[Q * q:Q * q + Q, PPG * g:PPG * g + PPG].rearrange("p i k c -> p (i k) c"),
                    weight[GROUP * g:GROUP * g + GROUP, DQ * q:DQ * q + DQ].rearrange("(k p) c -> p k c", p=Q),
                ).then_inc(w_landed[PPG * g], 16)

        def load_w_panel(eng, i):
            for q in range(NQ):
                eng.dma_start(
                    w_raw[Q * q:Q * q + Q, i],
                    weight[P * i:P * i + P, DQ * q:DQ * q + DQ].rearrange("(k p) c -> p k c", p=Q),
                ).then_inc(w_landed[i], 16)

        @block.sync
        def _(sp):
            def adapters(t):
                return [sp.value_load(ids_ok[0:1, bass.ds(SPT * t + s, 1)], min_val=0, max_val=NADAPT - 1)
                        for s in range(SPT)]

            def load_x(t, b):
                if from_tile(2, t):
                    sp.wait_ge(x_is_turned, t - 1)
                for q in range(NQ):
                    sp.dma_start(
                        x_raw[Q * q:Q * q + Q, b],
                        x_rows[bass.ds(P * t, P), DQ * q:DQ * q + DQ].rearrange("(k p) c -> p k c", p=Q),
                    ).then_inc(x_landed[b], 16)

            def load_a(t, b):
                chosen = adapters(t)
                if from_tile(2, t):
                    sp.wait_ge(a_is_turned, t - 1)
                for s in range(SPT):
                    sp.dma_start(
                        a_raw[:, b, s, :],
                        lora_a[bass.ds(chosen[s], 1)].rearrange("a r (v c) -> (a v) r c", c=R * D // P),
                    ).then_inc(a_landed[b], 16)

            def load_b(t, b):
                chosen = adapters(t)
                if from_tile(2, t):
                    sp.wait_ge(b_is_turned, t - 1)
                for s in range(SPT):
                    sp.dma_start(
                        b_raw[:, b, s, :],
                        lora_b[bass.ds(chosen[s], 1)].rearrange("a (p o) r -> (a p) (o r)", p=Q),
                    ).then_inc(b_landed[b], 16)

            def store(t, b):
                sp.wait_ge(result_ready, t + 1)
                sp.dma_start(out_rows[bass.ds(P * t, P), :], result[:, b, :]).then_inc(stored[b], 16)

            load_x(0, 0)
            load_w_panel(sp, PANEL_ORDER[1])
            sp.dma_start(ids_in[:, :], ids.rearrange("(a n) -> a n", a=1)).then_inc(ids_landed, 16)
            load_x(1, 1)
            load_w(sp, GROUP_ORDER[1])
            load_w(sp, GROUP_ORDER[2])
            sp.wait_ge(ids_step, 4)
            load_a(0, 0)
            load_a(1, 1)
            load_w(sp, GROUP_ORDER[3])
            load_b(0, 0)
            load_b(1, 1)
            sp.dma_start(bias_all[:, :], bias.rearrange("(a n) -> a n", a=1).to_broadcast([P, DOUT])
                         ).then_inc(bias_landed, 16)
            load_x(2, 0)
            load_x(3, 1)
            load_a(2, 0)
            load_a(3, 1)
            load_b(2, 0)
            store(0, 0)

            def step(t, b, pair, two_more):
                if two_more:
                    load_x(t + 2, b)
                    load_a(t + 2, b)
                load_b(t + 1, 1 - b)
                store(t - 1, 1 - b)

            steps(sp, step)
            store(TILES - 2, 0)
            for i, n in enumerate(LAST_ORDER):
                cols = slice(PIECES[1][n][2], PIECES[1][n][2] + OUT_N[n])
                sp.wait_ge(last_bank_ready, i + 1)
                sp.dma_start(out_rows[P * (TILES - 1):P * TILES, cols], result[:, 1, cols]).then_inc(stored_last, 16)
            sp.wait_ge(stored_last, 16 * len(LAST_ORDER))
            for b in range(2):
                sp.wait_ge(stored[b], 16 * (TILES // 2 - b))

        @block.gpsimd
        def _(pool):
            nc.gpsimd.memset(warm[:, 0:1], 0.0).then_inc(warm_zeroed, 1)
            for tile in (ident, ident32):
                nc.gpsimd.memset(tile[:, :], 0.0).then_inc(zeroed, 1)
            nc.gpsimd.memset(h_split[:, :, :].bitcast(F32), 0.0).then_inc(h_zeroed, 1)
            pool.wait_ge(zeroed, 2)
            for q in range(NQ):
                nc.gpsimd.affine_select(out=ident32[:, :], in_=ident32[:, :], compare_op=ALU.not_equal,
                                        fill=1.0, base=-Q * q, pattern=[[-1, Q]],
                                        channel_multiplier=1).then_inc(ident_ready, 1)
                pool.wait_ge(ident_ready, q + 1)
            nc.gpsimd.affine_select(out=ident[:, :], in_=ident[:, :], compare_op=ALU.not_equal, fill=1.0,
                                    base=0, pattern=[[-1, P]], channel_multiplier=1).then_inc(ident_ready, 1)
            pool.wait_ge(ident_ready, NQ + 1)

            def add_identity(n):
                i = PANEL_ORDER[n]
                q, c = P * i // DQ, P * i % DQ
                for k in range(XB):
                    diagonal = w_raw[Q * q:Q * q + Q, i, k, c + Q * k:c + Q * k + Q]
                    nc.gpsimd.tensor_tensor(diagonal, diagonal, ident32[Q * q:Q * q + Q, :],
                                            ALU.add).then_inc(w_plus_i, 1)

            def add_group_identity(g):
                pool.wait_ge(w_landed[PPG * GROUP_ORDER[g]], 16 * NQ)
                for n in range(PPG * g, PPG * g + PPG):
                    add_identity(n)

            def low_w(n):
                pool.wait_ge(w_high_ready, n + 1)
                cols = slice(at(P * PANEL_ORDER[n]), at(P * PANEL_ORDER[n]) + P)
                nc.gpsimd.tensor_tensor(w_low[:, :, cols], w_turned[:, n % WBUFS], w_high[:, :, cols].bitcast(F32),
                                        ALU.subtract).then_inc(w_ready_pool, 1)

            def panels_with_identity(n):
                pool.wait_ge(w_plus_i, XB * n)

            pool.wait_ge(w_landed[PANEL_ORDER[0]], 16 * NQ)
            add_identity(0)
            pool.wait_ge(w_landed[PANEL_ORDER[1]], 16 * NQ)
            add_identity(1)
            panels_with_identity(2)
            pool.wait_ge(ids_landed, 16)
            nc.gpsimd.tensor_copy(ids_f[:, :], ids_in[:, :]).then_inc(ids_step, 1)
            pool.wait_ge(ids_step, 1)
            nc.gpsimd.tensor_scalar(ids_neg[:, :], ids_f[:, :], 0.0, float(NADAPT), ALU.is_lt, ALU.mult).then_inc(ids_step, 1)
            pool.wait_ge(ids_step, 2)
            nc.gpsimd.tensor_tensor(ids_f[:, :], ids_f[:, :], ids_neg[:, :], ALU.add).then_inc(ids_step, 1)
            pool.wait_ge(ids_step, 3)
            nc.gpsimd.tensor_scalar(ids_ok[:, :], ids_f[:, :], 0.0, float(NADAPT - 1), ALU.max, ALU.min).then_inc(ids_step, 1)
            pool.wait_ge(ids_step, 4)
            add_group_identity(1)
            panels_with_identity(4)
            add_group_identity(2)
            panels_with_identity(6)
            add_group_identity(3)
            panels_with_identity(8)
            for n in POOL_PANELS:
                low_w(n)

        @block.scalar
        def _(act):
            def high_x(t, b):
                act.wait_ge(x_is_turned, t + 1)
                if from_tile(2, t):
                    act.wait_ge(base_done, t - 1)
                nc.scalar.copy(x_split[:, b, 0], x_turned[:, :, :]).then_inc(x_high_ready, 1)

            def high_a(t, b):
                act.wait_ge(a_is_turned, t + 1)
                if from_tile(2, t):
                    act.wait_ge(base_done, t - 1)
                nc.scalar.copy(w_high[:, :, A_AT[b]:A_AT[b] + Q], a_turned[:, b]).then_inc(a_high_ready, 1)

            def high_b(t):
                act.wait_ge(b_is_turned, t + 1)
                if from_tile(1, t):
                    act.wait_ge(lora_done, t)
                nc.scalar.copy(b_moving[0:Q, :], b_turned[:, :])
                nc.scalar.copy(b_moving[Q:2 * Q, :], b_turned[:, :]).then_inc(b_high_ready, 1)

            def copy_h(t):
                act.wait_ge(h_is_turned, t + 1)
                nc.scalar.copy(h_stat[0:3 * Q, :], h_turned[0:3 * Q, 0:P]).then_inc(h_stat_ready, 1)

            def high_w(n):
                i = PANEL_ORDER[n]
                act.wait_ge(w_is_turned, n + 1)
                nc.scalar.copy(w_high[:, :, at(P * i):at(P * i) + P], w_turned[:, n % WBUFS]).then_inc(w_high_ready, 1)

            load_w_panel(act, PANEL_ORDER[0])
            act.wait_ge(warm_zeroed, 1)
            nc.scalar.copy(warm[:, 1:2], warm[:, 0:1])
            high_x(0, 0)
            high_w(0)
            high_w(1)
            high_x(1, 1)
            for n in range(2, NW):
                high_w(n)
                if n == 3:
                    high_a(0, 0)
                    high_a(1, 1)
            high_b(0)
            copy_h(0)
            high_x(2, 0)
            high_a(2, 0)
            high_b(1)

            def step(t, b, pair, two_more):
                high_x(t + 1, 1 - b)
                high_a(t + 1, 1 - b)
                copy_h(t - 1)
                high_b(t)

            steps(act, step)
            copy_h(TILES - 2)
            high_b(TILES - 1)
            copy_h(TILES - 1)

        @block.tensor
        def _(pe):
            PASSES = ((0, w_high), (0, w_low), (1, w_high))

            def turn_h(t):
                pe.wait_ge(h_split_ready, t + 1)
                nc.tensor.transpose(h_turned[0:3 * Q, 0:P],
                                    h_split[:, :, :].bitcast(F32).rearrange("p a c -> p (a c)"),
                                    ident[:, :]).then_inc(h_is_turned, 1)

            def lora_bank(b, n):
                _, _, first, begin = PIECES[b][n]
                return nc.tensor.matmul(acc[b][n][:, begin:begin + OUT_N[n]], h_stat[0:3 * Q, :],
                                        b_moving[0:3 * Q, first:first + OUT_N[n]],
                                        start=False, stop=True, skip_group_check=True)

            def lora(t, b):
                pe.wait_ge(h_stat_ready, t + 1)
                pe.wait_ge(b_ready, t + 1)
                for n in range(3):
                    mm = lora_bank(b, n)
                mm.then_inc(lora_done, 1)

            def group(g, t):
                n = {0: 0, 1: 0, 2: 1, 3: 2}[g]
                col, width = (PIECES[t][2][0:2] if g == NG - 1 else (GROUP * g, GROUP))
                begin = GROUP * (g % 2) if n == 0 else 0
                for k in range(KT):
                    for part, w in PASSES:
                        mm = nc.tensor.matmul(acc[t][n][:, begin:begin + width], x_split[:, t, part, k, :],
                                              w[:, k, col:col + width],
                                              start=(begin == 0 and k == 0 and part == 0 and w is w_high),
                                              stop=False, skip_group_check=True)
                return mm

            def w_group_ready(g):
                by_pool = sum(n < PPG * (g + 1) for n in POOL_PANELS)
                pe.wait_ge(w_ready, PPG * (g + 1) - by_pool)
                if by_pool:
                    pe.wait_ge(w_ready_pool, by_pool)

            w_group_ready(0)
            for t in range(2):
                pe.wait_ge(x_ready, t + 1)
                group(GROUP_ORDER[0], t)
            w_group_ready(1)
            for t in range(2):
                pe.wait_ge(a_ready, t + 1)
                group(GROUP_ORDER[1], t).then_inc(h_done, 1)
            w_group_ready(2)
            group(GROUP_ORDER[2], 0)
            group(GROUP_ORDER[2], 1)
            pe.wait_ge(ident_ready, NQ + 1)
            turn_h(0)
            w_group_ready(3)
            group(GROUP_ORDER[3], 0).then_inc(base_done, 1)
            lora(0, 0)
            group(GROUP_ORDER[3], 1).then_inc(base_done, 1)

            def step(t, b, pair, two_more):
                pe.wait_ge(x_ready, t + 1)
                pe.wait_ge(a_ready, t + 1)
                pe.wait_ge(result_ready, t - 1)
                for k in range(KT):
                    for part, w in PASSES:
                        for n, (col, width, _, _) in enumerate(PIECES[b]):
                            mm = nc.tensor.matmul(acc[b][n][:, 0:width], x_split[:, b, part, k, :],
                                                  w[:, k, col:col + width],
                                                  start=(k == 0 and part == 0 and w is w_high),
                                                  stop=False, skip_group_check=True)
                    if k == KT - 1:
                        mm.then_inc(base_done, 1)
                    if k == 2:
                        turn_h(t - 1)
                    if k == 4:
                        lora(t - 1, 1 - b)

            steps(pe, step)

            pe.wait_ge(x_ready, TILES)
            pe.wait_ge(a_ready, TILES)
            pe.wait_ge(result_ready, TILES - 2)
            for i, n in enumerate(LAST_ORDER):
                col, width = PIECES[1][n][0:2]
                for k in range(KT):
                    for part, w in PASSES:
                        mm = nc.tensor.matmul(acc[1][n][:, 0:width], x_split[:, 1, part, k, :],
                                              w[:, k, col:col + width],
                                              start=(k == 0 and part == 0 and w is w_high),
                                              stop=False, skip_group_check=True)
                    if i == 1 and k == 1:
                        lora(TILES - 2, 0)
                    if i == 1 and k == 3:
                        turn_h(TILES - 1)
                    if i == 2 and k == 1:
                        pe.wait_ge(h_stat_ready, TILES)
                        pe.wait_ge(b_ready, TILES)
                        for done in LAST_ORDER[0:2]:
                            lora_bank(1, done).then_inc(last_bank_done, 1)
                if i == 0:
                    mm.then_inc(h_done, 1)
                    turn_h(TILES - 2)
            lora_bank(1, LAST_ORDER[2]).then_inc(last_bank_done, 1)

        @block.vector
        def _(dve):
            def turn_x(t, b, landed):
                dve.wait_ge(x_landed[b], 16 * NQ * landed)
                if from_tile(1, t):
                    dve.wait_ge(x_ready, t)
                nc.vector.transpose(
                    x_turned[:, :, :].rearrange("p j (k c) -> p k j c", c=Q),
                    x_raw[:, b].rearrange("p k (j c) -> p k j c", c=Q),
                ).then_inc(x_is_turned, 1)

            def low_x(t, b):
                dve.wait_ge(x_high_ready, t + 1)
                nc.vector.tensor_tensor(x_split[:, b, 1], x_turned[:, :, :], x_split[:, b, 0].bitcast(F32),
                                        ALU.subtract).then_inc(x_ready, 1)

            def turn_a(t, b, landed):
                dve.wait_ge(a_landed[b], 16 * SPT * landed)
                if from_tile(2, t):
                    dve.wait_ge(a_ready, t - 1)
                turned = a_turned[:, b].rearrange("p (u j) (s r) -> p s j u r", u=Q // R, s=SPT)
                for s in range(SPT):
                    ins = nc.vector.transpose(turned[:, s], a_raw[:, b, s, :])
                ins.then_inc(a_is_turned, 1)

            def low_a(t, b):
                dve.wait_ge(a_high_ready, t + 1)
                cols = slice(A_AT[b], A_AT[b] + Q)
                nc.vector.tensor_tensor(w_low[:, :, cols], a_turned[:, b], w_high[:, :, cols].bitcast(F32),
                                        ALU.subtract).then_inc(a_ready, 1)

            def split_h(t, b):
                if isinstance(t, int) and t in FIRST_H:
                    dve.wait_ge(h_done, FIRST_H.index(t) + 1)
                else:
                    dve.wait_ge(base_done, t + 1)
                if from_tile(1, t):
                    dve.wait_ge(h_is_turned, t)

                def own(s):
                    own_h = acc[b][2][S * s:S * s + S, H_AT[b] + R * s:H_AT[b] + R * s + R]
                    return own_h, h_split[S * s:S * s + S, :, R * s:R * s + R]

                for s in range(SPT):
                    own_h, parts = own(s)
                    for part in (0, 2):
                        nc.vector.tensor_copy(parts[:, part, :], own_h).then_inc(h_high_ready, 1)
                dve.wait_ge(h_high_ready, 2 * SPT * (t + 1))
                for s in range(SPT):
                    own_h, parts = own(s)
                    ins = nc.vector.tensor_tensor(parts[:, 1, :], own_h, parts[:, 0, :].bitcast(F32), ALU.subtract)
                ins.then_inc(h_split_ready, 1)

            def turn_b(t, b, landed):
                dve.wait_ge(b_landed[b], 16 * SPT * landed)
                if from_tile(1, t):
                    dve.wait_ge(b_ready, t)
                nc.vector.transpose(
                    b_turned[:, :].rearrange("p (c o) -> p o c", c=Q),
                    b_raw[:, b].rearrange("p s (o r) -> p o s r", r=R),
                ).then_inc(b_is_turned, 1)

            def low_b(t):
                dve.wait_ge(b_high_ready, t + 1)
                nc.vector.tensor_tensor(b_moving[2 * Q:3 * Q, :], b_turned[:, :], b_moving[0:Q, :].bitcast(F32),
                                        ALU.subtract).then_inc(b_ready, 1)

            def finish_bank(b, n):
                _, _, first, begin = PIECES[b][n]
                cols = slice(first, first + OUT_N[n])
                return nc.vector.tensor_tensor(result[:, b, cols], acc[b][n][:, begin:begin + OUT_N[n]],
                                               bias_all[:, cols], ALU.add)

            def finish(t, b, landed):
                dve.wait_ge(lora_done, t + 1)
                if from_tile(2, t):
                    dve.wait_ge(stored[b], 16 * landed)
                for n in range(3):
                    ins = finish_bank(b, n)
                ins.then_inc(result_ready, 1)

            def turn_w(n):
                i = PANEL_ORDER[n]
                dve.wait_ge(w_plus_i, XB * (n + 1))
                if n >= WBUFS:
                    dve.wait_ge(w_ready, n - WBUFS + 1)
                nc.vector.transpose(
                    w_turned[:, n % WBUFS].rearrange("p j (k c) -> p k j c", c=Q),
                    w_raw[:, i].rearrange("p k (j c) -> p k j c", c=Q),
                ).then_inc(w_is_turned, 1)

            def low_w(n):
                i = PANEL_ORDER[n]
                dve.wait_ge(w_high_ready, n + 1)
                cols = slice(at(P * i), at(P * i) + P)
                nc.vector.tensor_tensor(w_low[:, :, cols], w_turned[:, n % WBUFS], w_high[:, :, cols].bitcast(F32),
                                        ALU.subtract).then_inc(w_ready, 1)

            turn_x(0, 0, 1)
            turn_w(0)
            low_x(0, 0)
            turn_w(1)
            low_w(0)
            low_w(1)
            turn_x(1, 1, 1)
            turn_w(2)
            low_x(1, 1)
            turn_w(3)
            turn_a(0, 0, 1)
            turn_a(1, 1, 1)
            low_w(2)
            low_w(3)
            low_a(0, 0)
            low_a(1, 1)
            turn_w(4)
            turn_w(5)
            low_w(4)
            turn_w(6)
            turn_w(7)
            low_w(6)
            dve.wait_ge(h_zeroed, 1)
            split_h(0, 0)
            turn_b(0, 0, 1)
            low_b(0)
            turn_x(2, 0, 2)
            turn_a(2, 0, 2)
            turn_b(1, 1, 1)
            dve.wait_ge(bias_landed, 16)
            finish(0, 0, 0)
            low_x(2, 0)
            low_a(2, 0)
            low_b(1)

            def step(t, b, pair, two_more):
                split_h(t - 1, 1 - b)
                turn_x(t + 1, 1 - b, pair + 1 + b)
                turn_a(t + 1, 1 - b, pair + 1 + b)
                low_x(t + 1, 1 - b)
                low_a(t + 1, 1 - b)
                finish(t - 1, 1 - b, pair - 1 + b)
                turn_b(t, b, pair + 1)
                low_b(t)

            steps(dve, step)
            split_h(TILES - 2, 0)
            split_h(TILES - 1, 1)
            turn_b(TILES - 1, 1, TILES // 2)
            low_b(TILES - 1)
            finish(TILES - 2, 0, TILES // 2 - 1)
            dve.wait_ge(stored[1], 16 * (TILES // 2 - 1))
            for i, n in enumerate(LAST_ORDER):
                dve.wait_ge(last_bank_done, i + 1)
                finish_bank(1, n).then_inc(last_bank_ready, 1)


_INS = ["x", "itok_B_6_15", "L0_cond_base_weight", "L0_cond_base_bias", "L0_cond_lora_A_w", "L0_cond_lora_B_w"]


def kernel(**inputs):
    import numpy as np
    import concourse.bacc as bacc
    from concourse.bass_utils import run_bass_kernel_spmd

    nc = bacc.Bacc("TRN2", target_bir_lowering=False, num_devices=1)
    arrays, args = {}, []
    for name in _INS:
        a = np.ascontiguousarray(inputs[name])
        arrays[f"in_{name}"] = a
        args.append(nc.dram_tensor(f"in_{name}", a.shape, mybir.dt.from_np(a.dtype), kind="ExternalInput").ap())
    shape = arrays["in_x"].shape
    args.append(nc.dram_tensor("out", shape, F32, kind="ExternalOutput").ap())
    lora_residual(nc, *args)
    ran = run_bass_kernel_spmd(nc, [arrays], core_ids=[0])
    return ran.results[0]["out"]
```
